# Optimizing a Trainium2 kernel written in Bass

```python
import numpy as np
import jax
import jax.numpy as jnp

def _softmax(x, axis=-1):
    return jax.nn.softmax(x, axis=axis)

def _gelu(x):
    return jax.nn.gelu(x, approximate=True)

def _silu(x):
    return jax.nn.silu(x)

def _sigmoid(x):
    return jax.nn.sigmoid(x)

def _layernorm(x, axis=-1, eps=1e-05):
    m = jnp.mean(x, axis=axis, keepdims=True)
    v = jnp.var(x, axis=axis, keepdims=True)
    return (x - m) / jnp.sqrt(v + eps)

def _scatter_add(tgt, idx, src, axis=0):
    return tgt.at[idx].add(src)

def _segment_sum(src, seg, n):
    return jax.ops.segment_sum(src, seg, n)
kernel_name = 'mk_cond_resid_d2_seqx_r2_bf9d70'

def setup_inputs(seed: int=0):
    np.random.seed(seed)
    _w = jnp.asarray

    def _rec_inputs():
        import jax
        import jax.numpy as jnp
        _rk = jax.random.key(seed)
        x = -0.0003929 + 0.9999 * jax.random.normal(jax.random.fold_in(_rk, 1), (2, 2048, 512), jnp.float32)
        _lenS = 2048 - jax.random.randint(jax.random.fold_in(_rk, 7), (2,), 0, max(1, 2048 // 4) + 1, jnp.int32)
        _lenS2 = 2048 - jax.random.randint(jax.random.fold_in(_rk, 8), (2,), 0, max(1, 2048 // 4) + 1, jnp.int32)
        cond_1024 = 0.00782532 + 1.00527 * jax.random.normal(jax.random.fold_in(_rk, 11), (2, 512), jnp.float32)
        return (x, cond_1024)
    x, cond_1024 = _rec_inputs()

    def _L0_cond_setup():
        import jax, jax.numpy as jnp
        import numpy as np
        EPS = 1e-08
        key = jax.random.key(seed)
        ks = jax.random.split(key, 8)
        B, S, D, H = (8, 1024, 512, 512)
        scale = 1.0 / np.sqrt(D)
        return {'input_seq': jax.random.normal(ks[0], (B, S, D), dtype=jnp.float32), 'initial_hidden': jax.random.normal(ks[1], (B, H), dtype=jnp.float32), 'W_f': jax.random.normal(ks[2], (H, D), dtype=jnp.float32) * scale, 'b_f': jnp.zeros((H,), dtype=jnp.float32), 'W_i': jax.random.normal(ks[3], (H, D), dtype=jnp.float32) * scale, 'b_i': jnp.zeros((H,), dtype=jnp.float32), 'W_h': jax.random.normal(ks[4], (H, D), dtype=jnp.float32) * scale, 'b_h': jnp.zeros((H,), dtype=jnp.float32)}
    _L0_cond_all = _L0_cond_setup()
    _L0_cond_in = {k: v for k, v in _L0_cond_all.items() if k in ('W_f', 'b_f', 'W_i', 'b_i', 'W_h', 'b_h')}
    del _L0_cond_all

    def _L1_cond_setup():
        import jax, jax.numpy as jnp
        import numpy as np
        N, T, D, H = (64, 256, 512, 512)

        def lstm_scan(x, h0, Wx, Wh, b):
            xW = jnp.einsum('ntd,dg->ntg', x, Wx) + b
            Hdim = h0.shape[1]
            c0 = jnp.zeros_like(h0)

            def step(carry, xw_t):
                prev_h, prev_c = carry
                a = xw_t + prev_h @ Wh
                i = jax.nn.sigmoid(a[:, :Hdim])
                f = jax.nn.sigmoid(a[:, Hdim:2 * Hdim])
                o = jax.nn.sigmoid(a[:, 2 * Hdim:3 * Hdim])
                g = jnp.tanh(a[:, 3 * Hdim:])
                next_c = f * prev_c + i * g
                next_h = o * jnp.tanh(next_c)
                return ((next_h, next_c), next_h)
            _, hs = jax.lax.scan(step, (h0, c0), jnp.swapaxes(xW, 0, 1))
            return jnp.swapaxes(hs, 0, 1)
        key = jax.random.key(seed)
        k1, k2, k3, k4 = jax.random.split(key, 4)
        x = jax.random.normal(k1, (N, T, D), dtype=jnp.float32)
        h0 = jax.random.normal(k2, (N, H), dtype=jnp.float32)
        Wx = jax.random.normal(k3, (D, 4 * H), dtype=jnp.float32) / np.sqrt(D)
        Wh = jax.random.normal(k4, (H, 4 * H), dtype=jnp.float32) / np.sqrt(H)
        b = jnp.zeros((4 * H,), dtype=jnp.float32)
        return {'x': x, 'h0': h0, 'Wx': Wx, 'Wh': Wh, 'b': b}
    _L1_cond_all = _L1_cond_setup()
    _L1_cond_in = {k: v for k, v in _L1_cond_all.items() if k in ('Wx', 'Wh', 'b')}
    del _L1_cond_all
    return {'x': x, 'cond_1024': cond_1024, 'L0_cond_W_f': _L0_cond_in['W_f'], 'L0_cond_b_f': _L0_cond_in['b_f'], 'L0_cond_W_i': _L0_cond_in['W_i'], 'L0_cond_b_i': _L0_cond_in['b_i'], 'L0_cond_W_h': _L0_cond_in['W_h'], 'L0_cond_b_h': _L0_cond_in['b_h'], 'L1_cond_Wx': _L1_cond_in['Wx'], 'L1_cond_Wh': _L1_cond_in['Wh'], 'L1_cond_b': _L1_cond_in['b']}

def reference(x, cond_1024, L0_cond_W_f, L0_cond_b_f, L0_cond_W_i, L0_cond_b_i, L0_cond_W_h, L0_cond_b_h, L1_cond_Wx, L1_cond_Wh, L1_cond_b):
    import jax
    import jax.numpy as jnp

    def _L0_cond_ref(input_seq, initial_hidden, W_f, b_f, W_i, b_i, W_h, b_h):
        import jax, jax.numpy as jnp
        import numpy as np
        EPS = 1e-08
        forget_gate = jax.nn.sigmoid(jnp.einsum('bsd,hd->bsh', input_seq, W_f) + b_f)
        input_gate = jax.nn.sigmoid(jnp.einsum('bsd,hd->bsh', input_seq, W_i) + b_i)
        gate_sum = forget_gate + input_gate + EPS
        forget_norm = forget_gate / gate_sum
        input_norm = input_gate / gate_sum
        candidate = jnp.einsum('bsd,hd->bsh', input_seq, W_h) + b_h
        new_info = input_norm * candidate
        log_ret = jnp.log(forget_norm + EPS)
        log_cumprod = jnp.cumsum(log_ret, axis=1)
        B, _, H = log_cumprod.shape
        padded = jnp.concatenate([jnp.zeros((B, 1, H), dtype=log_cumprod.dtype), log_cumprod], axis=1)
        scaling = jnp.exp(log_cumprod[:, -1:, :] - padded[:, :-1, :])
        hidden = jnp.cumsum(scaling * new_info, axis=1)
        hidden = hidden + jnp.exp(log_cumprod) * initial_hidden[:, None, :]
        return hidden

    def _L1_cond_ref(x, h0, Wx, Wh, b):
        import jax, jax.numpy as jnp
        import numpy as np
        N, T, D, H = (64, 256, 512, 512)

        def lstm_scan(x, h0, Wx, Wh, b):
            xW = jnp.einsum('ntd,dg->ntg', x, Wx) + b
            Hdim = h0.shape[1]
            c0 = jnp.zeros_like(h0)

            def step(carry, xw_t):
                prev_h, prev_c = carry
                a = xw_t + prev_h @ Wh
                i = jax.nn.sigmoid(a[:, :Hdim])
                f = jax.nn.sigmoid(a[:, Hdim:2 * Hdim])
                o = jax.nn.sigmoid(a[:, 2 * Hdim:3 * Hdim])
                g = jnp.tanh(a[:, 3 * Hdim:])
                next_c = f * prev_c + i * g
                next_h = o * jnp.tanh(next_c)
                return ((next_h, next_c), next_h)
            _, hs = jax.lax.scan(step, (h0, c0), jnp.swapaxes(xW, 0, 1))
            return jnp.swapaxes(hs, 0, 1)
        return lstm_scan(x, h0, Wx, Wh, b)
    x = x + _L0_cond_ref(x, cond_1024, L0_cond_W_f, L0_cond_b_f, L0_cond_W_i, L0_cond_b_i, L0_cond_W_h, L0_cond_b_h)
    x = x + _L1_cond_ref(x, cond_1024, L1_cond_Wx, L1_cond_Wh, L1_cond_b)
    return x

_drawn_inputs = setup_inputs


def setup_inputs(seed=0):
    import zlib

    import numpy as np

    out = dict(_drawn_inputs(seed))
    spreads = {'L0_cond_b_f': (0.0, 0.8),
     'L0_cond_b_i': (0.0, 0.8),
     'L0_cond_b_h': (0.0, 0.8),
     'L1_cond_b': (0.0, 0.1)}
    factors = {'cond_1024': 3.91, 'L0_cond_W_f': 8.0, 'L0_cond_W_i': 8.0, 'L0_cond_W_h': 8.0}
    for name, (base, spread) in spreads.items():
        noise = np.random.default_rng([zlib.crc32(name.encode()), seed]).standard_normal(out[name].shape)
        drawn = base * np.exp(spread * noise) if base else spread * noise
        out[name] = jnp.asarray(drawn.astype(out[name].dtype))
    for name, factor in factors.items():
        out[name] = (out[name] * factor).astype(out[name].dtype)
    return out
```

```python
from contextlib import ExitStack

import concourse.bass as bass
from concourse import mybir

F32 = mybir.dt.float32
F16 = mybir.dt.float16
BF16 = mybir.dt.bfloat16
I32 = mybir.dt.int32
ALU = mybir.AluOpType
ACT = mybir.ActivationFunctionType
AX = mybir.AxisListType
RMAX = bass.bass_isa.ReduceOp.max

P = 128
BATCH, SEQ, D = 2, 2048, 512
NK = D // P
GATES = 4
NMG = NK * GATES
EPS = 1e-8

TC = 512
NTC = SEQ // TC
NW = 3
TILES = SEQ // P
XSLOTS = 8

CHUNK = 256
NCHUNK = SEQ // CHUNK
HALF = 4
BLOCK = 2 * HALF
NBLOCK = CHUNK // BLOCK
XW_STEP = GATES * BATCH
XW_PART = CHUNK * XW_STEP
XW_PAD = HALF * XW_STEP
NPART = 3
N_VEC = NW * NK + NMG + BATCH * NK
H_SCALE = 4096.0
G_COLS = 2 * BATCH
S_COLS = GATES * G_COLS

PE_ORDER = [(0, 0), (0, 1), (0, 2), (1, 0), (1, 1), (2, 0), (2, 1), (0, 3),
            (3, 0), (3, 1), (1, 2), (2, 2), (3, 2), (1, 3), (2, 3), (3, 3)]
DVE_ORDER = [("sum", 0), ("sum", 1), ("mul", 0), ("cell", 0), ("mul", 1), ("sum", 2), ("cell", 1),
             ("high", 0), ("h", 0), ("mul", 2), ("high", 1), ("low", 0), ("sum", 3), ("h", 1),
             ("cell", 2), ("low", 1), ("mul", 3), ("high", 2), ("h", 2), ("cell", 3), ("low", 2),
             ("high", 3), ("h", 3), ("low", 3)]
ACT_ORDER = [("cand", 0), ("sig", 0), ("cand", 1), ("sig", 1), ("tanh", 0), ("cand", 2),
             ("sig", 2), ("tanh", 1), ("cand", 3), ("sig", 3), ("tanh", 2), ("tanh", 3)]
LAST = {m: max(i for i, (_, mm) in enumerate(PE_ORDER) if mm == m) for m in range(NK)}
PE_DONE = sorted(range(NK), key=LAST.get)


def build(nc, x, cond, w_f, b_f, w_i, b_i, w_h, b_h, wx, wh, b1, out):
    ctx = ExitStack()
    with ctx:
        def sb(name, shape, dt):
            return ctx.enter_context(nc.sbuf_tensor(name, shape, dt))

        def sem(name):
            return ctx.enter_context(nc.semaphore(name))

        xT = sb("xT", [P, NK, BATCH, SEQ], F32)
        wx_sb = sb("wx_sb", [P, NK, GATES * D], F32)
        wh_parts = sb("wh_parts", [P, NK * NMG * 2 * P], F16)
        work = sb("work", [P, 12672], F32)
        small8 = sb("small8", [P, 2048], F32)
        pair_a = sb("pair_a", [P, 2, TC], F32)
        pair_b = sb("pair_b", [P, 2, TC], F32)
        rows8 = sb("rows8", [P, NK, D], F32)
        identf = sb("identf", [P, P], F32)
        identb = sb("identb", [P, P], BF16)
        vec_rows = sb("vec_rows", [N_VEC, P], F32)
        vecT = sb("vecT", [P, N_VEC], F32)
        bias1_scaled = sb("bias1_scaled", [P, GATES, NK], F32)
        scales = sb("scales", [P, 8], F32)
        h0_gates = sb("h0_gates", [P, NMG, BATCH], F32)

        biasT = vecT[:, 0:NW * NK].rearrange("p (w k) -> p w k", w=NW)
        bias1T = vecT[:, NW * NK:NW * NK + NMG].rearrange("p (g m) -> p g m", g=GATES)
        h0T = vecT[:, NW * NK + NMG:N_VEC].rearrange("p (b k) -> p b k", b=BATCH)

        wT = work[:, 0:NK * NW * D].rearrange("p (k w h) -> p k w h", k=NK, w=NW)
        ret = work[:, 6144:8192]
        new_info = work[:, 8192:10240]
        scaling = work[:, 10240:12288]
        hidden = wh_parts[:, :].bitcast(F32).rearrange("p (k t) -> p k t", k=NK)
        forget = small8[:, 0:2 * TC].rearrange("p (n t) -> p n t", n=2)
        inp = small8[:, 2 * TC:4 * TC].rearrange("p (n t) -> p n t", n=2)
        gate_sum, recip = pair_a[:, 0, :], pair_a[:, 1, :]
        forget_norm, input_norm = pair_b[:, 0, :], pair_b[:, 1, :]
        prefix = rows8[:, :, :].rearrange("p a b -> p (a b)")
        wh_f32 = wx_sb

        whp = wh_parts[:, :].rearrange("p (k n s j) -> p k n s j", k=NK, n=NMG, s=2)
        xw = work[:, :].bitcast(BF16)[:, 0:NK * NPART * (XW_PART + XW_PAD)]\
            .rearrange("p (m s c) -> p m s c", m=NK, s=NPART)
        hist = small8[:, :].rearrange("p (k b t) -> p k b t", k=NK, b=BATCH)
        h_parts = sb("h_parts", [P, 2, NK, G_COLS], F16)
        xs = sb("xs", [P, NK, NPART, XW_PAD], BF16)
        pre = sb("pre", [P, NK, XW_STEP], F32)
        gc = sb("gc", [P, NK, (GATES + 1) * BATCH], F32)
        uv = sb("uv", [P, NK, 2 * BATCH], F32)
        tanh_c = sb("tanh_c", [P, NK, BATCH], F32)
        h_half = sb("h_half", [P, 2, NK, BATCH, HALF], F32)
        scrap = sb("scrap", [P, 16], F32)

        ps = ctx.enter_context(nc.psum_tensor("ps", [P, 2, NK, 512], F32))
        ps8 = ps[:, :, :, :].rearrange("p s m c -> p (s m) c")

        consts = sem("consts")
        small_in = sem("small_in")
        w_in = [sem(f"w_in{w}") for w in range(NW)]
        x_in = [sem(f"x_in{s}") for s in range(BATCH * TILES // 4)]
        wh_in = sem("wh_in")
        wx_in = [sem(f"wx_in{k}") for k in range(NK)]
        vec_turned = sem("vec_turned")
        vec_ready = sem("vec_ready")
        turned = sem("turned")
        stored_act = sem("stored_act")
        stored_dve = sem("stored_dve")
        l0_products = sem("l0_products")
        l0_gates = sem("l0_gates")
        l0_recip = sem("l0_recip")
        l0_forget = sem("l0_forget")
        l0_ret = sem("l0_ret")
        l0_info = sem("l0_info")
        l0_step = sem("l0_step")
        l0_x1 = sem("l0_x1")
        wh_max = sem("wh_max")
        wh_max_all = sem("wh_max_all")
        scale_step = sem("scale_step")
        scales_ready = sem("scales_ready")
        wh_high = sem("wh_high")
        wh_low = sem("wh_low")
        h0_product = sem("h0_product")
        h0_ready = sem("h0_ready")
        state_zero = sem("state_zero")
        xw_product = sem("xw_product")
        xw_full = sem("xw_full")
        xw_step = sem("xw_step")
        xw_ready = sem("xw_ready")
        xs_first = sem("xs_first")
        first_added = sem("first_added")
        pool_passed = sem("pool_passed")
        y_ready = sem("y_ready")
        y_turned = sem("y_turned")
        y_rows = sem("y_rows")
        out_done = sem("out_done")
        pe_gates = [sem(f"pe_gates{s}") for s in range(2)]
        act_done = [sem(f"act_done{s}") for s in range(2)]
        dve_done = [sem(f"dve_done{s}") for s in range(2)]
        xs_added = [sem(f"xs_added{s}") for s in range(2)]
        pool_done = [sem(f"pool_done{s}") for s in range(2)]

        n_dve, n_act = len(DVE_ORDER), len(ACT_ORDER)

        def place(t):
            return (t % BLOCK) // HALF, t % HALF

        def wait_gates(eng, m, t):
            s, i = place(t)
            eng.wait_ge(pe_gates[s], i * NK + PE_DONE.index(m) + 1)

        def wait_act(eng, what, m, t):
            s, i = place(t)
            eng.wait_ge(act_done[s], i * n_act + ACT_ORDER.index((what, m)) + 1)

        def wait_dve(eng, what, m, t):
            s, i = place(t)
            eng.wait_ge(dve_done[s], i * n_dve + DVE_ORDER.index((what, m)) + 1)

        block = ctx.enter_context(nc.Block())

        @block.sync
        def _(sp):
            w_stage = wh_parts[:, :].bitcast(F32)[:, 0:NW * NK * D].rearrange("p (w c d) -> p w c d", w=NW, c=NK)
            for w, src in enumerate((w_f, w_i, w_h)):
                sp.dma_start(w_stage[:, w], src.rearrange("(c p) d -> p c d", p=P)).then_inc(w_in[w], 16)
            for n in range(BATCH * TILES // 4):
                b, q = divmod(n, TILES // 4)
                if n >= XSLOTS // 4:
                    sp.wait_ge(turned, NW * NK + 4 * (n - XSLOTS // 4 + 1))
                sp.dma_start(x_slots(work, n), x[b, q * 4 * P:(q + 1) * 4 * P, :]
                             .rearrange("(j p) d -> p j d", p=P)).then_inc(x_in[n], 16)
            sp.dma_start(wh_f32[:, :, :], wh.rearrange("(k p) n -> p k n", p=P)).then_inc(wh_in, 16)
            sp.wait_ge(h0_product, 1)
            for k in range(NK):
                sp.wait_ge(wh_low, k + 1)
                sp.dma_start(wx_sb[:, k, :], wx[k * P:(k + 1) * P, :]).then_inc(wx_in[k], 16)
            with sp.Fori(0, NCHUNK) as c:
                for q in range(4):
                    b, j = divmod(q, 2)
                    sp.wait_ge(y_rows, c * 4 + (q + 1) + 1)
                    sp.dma_start(out[b, bass.ds(c * CHUNK + j * P, P), :], rows8[:, q, :]).then_inc(out_done, 16)
            sp.wait_ge(out_done, NCHUNK * 4 * 16 + 16)

        @block.gpsimd
        def _(pool):
            for counted in (l0_ret, l0_forget, l0_info, l0_x1, y_turned, y_rows):
                pool.sem_inc(counted, 1)
            pool.sem_inc(out_done, 16)
            pool.memset(identf[:, :], 0.0).then_inc(consts, 1)
            pool.memset(identb[:, :], 0.0).then_inc(consts, 1)
            pool.wait_ge(consts, 2)
            for ident in (identf, identb):
                pool.affine_select(out=ident[:, :], in_=ident[:, :], compare_op=ALU.not_equal, fill=1.0,
                                   base=0, pattern=[[-1, P]], channel_multiplier=1).then_inc(consts, 1)
            pool.wait_ge(wh_max, 1)
            pool.partition_all_reduce(scales[:, 1:2], scales[:, 0:1], P, RMAX).then_inc(wh_max_all, 1)
            with pool.Fori(0, BATCH) as b:
                for n in range(NK * NTC):
                    pool.wait_ge(l0_recip, b * (NK * NTC) + (n + 1))
                    pool.wait_ge(l0_ret, b * (NK * NTC) + n + 1)
                    pool.tensor_tensor(forget_norm, forget[:, n % 2, :], recip, ALU.mult).then_inc(l0_forget, 1)
            with pool.Fori(0, NCHUNK) as c:
                pool.wait_ge(xw_ready, c * NMG + NMG)
                pool.sem_inc(pool_passed, 1)
                pool.tensor_copy(xs[:, :, :, :], xw[:, :, :, 0:XW_PAD]).then_inc(xs_first, 1)
                pool.wait_ge(first_added, c + 1)
                pool.wait_ge(y_turned, c * 4 + 1)
                pool.sem_inc(pool_passed, 1)
                with pool.Fori(0, NBLOCK) as blk:
                    for s in range(2):
                        pool.wait_ge(xs_added[1 - s], 1)
                        pool.tensor_copy(xs[:, :, :, :], xw[:, :, :, bass.ds(blk * (2 * XW_PAD) + (1 + s) * XW_PAD, XW_PAD)])\
                            .then_inc(pool_done[s], 1)
                        wait_dve(pool, "low", 3, s * HALF + HALF - 1)
                        pool.tensor_copy(hist[:, :, :, bass.ds(blk * BLOCK + s * HALF, HALF)],
                                         h_half[:, s]).then_inc(pool_done[s], 1)

        @block.scalar
        def _(act):
            for at, src in ((0, b_f), (NK, b_i), (2 * NK, b_h), (NW * NK, b1)):
                rows = src.shape[0] // P
                act.dma_start(vec_rows[at:at + rows, :], src.rearrange("(k p) -> k p", p=P)).then_inc(small_in, 16)
            act.dma_start(vec_rows[NW * NK + NMG:N_VEC, :], cond.rearrange("b (k p) -> (b k) p", p=P))\
               .then_inc(small_in, 16)
            for n in range(1, NW * NK + BATCH * TILES, 2):
                act.wait_ge(turned, n + 1)
                act.activation(turned_to(wT, xT, n), ps8[:, n % 8, :].rearrange("p (k t) -> p k t", k=NK),
                               ACT.Copy).then_inc(stored_act, 1)
            act.wait_ge(vec_turned, 1)
            act.activation(vecT[:, :], ps[:, 0, 0, 0:N_VEC], ACT.Copy).then_inc(vec_ready, 1)
            act.wait_ge(vec_ready, 1)
            with act.Fori(0, BATCH) as b:
                for n in range(NK * NTC):
                    m, q = divmod(n, NTC)
                    act.wait_ge(l0_products, b * (NK * NTC) + (n + 1))
                    if n >= 2:
                        act.wait_ge(l0_forget, b * (NK * NTC) + (n - 1) + 1)
                        act.wait_ge(l0_info, b * (NK * NTC) + (n - 1) + 1)
                    else:
                        act.wait_ge(l0_forget, b * (NK * NTC) + 1)
                        act.wait_ge(l0_info, b * (NK * NTC) + 1)
                    act.activation(forget[:, n % 2, :], ps[:, n % 2, 0, :], ACT.Sigmoid, bias=biasT[:, 0, m:m + 1])
                    act.activation(inp[:, n % 2, :], ps[:, n % 2, 1, :], ACT.Sigmoid, bias=biasT[:, 1, m:m + 1])\
                        .then_inc(l0_gates, 1)
                    act.wait_ge(l0_forget, b * (NK * NTC) + (n + 1) + 1)
                    if q == 0:
                        act.wait_ge(l0_x1, b * NK + m + 1)
                    act.activation(ret[:, q * TC:(q + 1) * TC], forget_norm, ACT.Copy, bias=EPS).then_inc(l0_ret, 1)
            act.wait_ge(scales_ready, 1)
            act.wait_ge(xw_step, BATCH * NK)
            for k in range(NK):
                act.activation(whp[:, k, :, 0, :],
                               wh_f32[:, k, :].rearrange("p (n j) -> p n j", n=NMG),
                               ACT.Copy, scale=scales[:, 4:5]).then_inc(wh_high, 1)
            act.wait_ge(h0_product, 1)
            act.activation(h0_gates[:, :, :], ps[:, 0, 0, 0:NMG * BATCH].rearrange("p (n b) -> p n b", b=BATCH),
                           ACT.Copy, scale=scales[:, 5:6]).then_inc(h0_ready, 1)
            unscale = act.alloc_register("unscale")
            act.reg_load(unscale, scales[0:1, 6:7].bitcast(I32))
            act.wait_ge(state_zero, 2)

            with act.Fori(0, NCHUNK) as c:
                for n in range(NMG):
                    act.wait_ge(xw_product, c * NMG + (n + 1))
                    if n >= 2:
                        act.wait_ge(xw_ready, c * NMG + (n - 1))
                    act.activation(pair_a[:, n % 2, :], ps[:, 1, n % 4, :], ACT.Identity,
                                   bias=bias1_scaled[:, n % GATES, n // GATES:n // GATES + 1], scale=scales[:, 5:6]).then_inc(xw_full, 1)
                with act.Fori(0, NBLOCK) as blk:
                    for t in range(BLOCK):
                        done = act_done[place(t)[0]]
                        for what, m in ACT_ORDER:
                            if what == "cand":
                                wait_dve(act, "sum", m, t)
                                act.activation(gc[:, m, 6:8], pre[:, m, 6:8], ACT.Tanh, scale=unscale)\
                                    .then_inc(done, 1)
                            elif what == "sig":
                                act.activation(gc[:, m, 0:6], pre[:, m, 0:6], ACT.Sigmoid, scale=unscale)\
                                    .then_inc(done, 1)
                            else:
                                wait_dve(act, "cell", m, t)
                                act.activation(tanh_c[:, m, :], gc[:, m, 8:10], ACT.Tanh).then_inc(done, 1)
                act.wait_ge(out_done, c * (4 * 16) + 16)
                for q in range(4):
                    act.wait_ge(y_turned, c * 4 + (q + 1) + 1)
                    act.activation(rows8[:, q, :], ps[:, 0, q, :], ACT.Copy).then_inc(y_rows, 1)

        @block.vector
        def _(dve):
            for n in range(0, NW * NK + BATCH * TILES, 2):
                dve.wait_ge(turned, n + 1)
                dve.tensor_copy(turned_to(wT, xT, n), ps8[:, n % 8, :].rearrange("p (k t) -> p k t", k=NK))\
                    .then_inc(stored_dve, 1)
            dve.wait_ge(wh_in, 16)
            dve.tensor_reduce(scales[:, 0:1], wh_f32[:, :, :], axis=AX.XY, op=ALU.max,
                              apply_absolute_value=True).then_inc(wh_max, 1)
            dve.wait_ge(wh_max_all, 1)
            dve.tensor_scalar(scales[:, 2:3], scales[:, 1:2], 2.0 ** -46, 2.0 ** 100, ALU.max, ALU.min)\
                .then_inc(scale_step, 1)
            dve.wait_ge(scale_step, 1)
            dve.tensor_single_scalar(scales[:, 2:3].bitcast(I32), scales[:, 2:3].bitcast(I32), 0x7F800000,
                                     ALU.bitwise_and).then_inc(scale_step, 1)
            dve.wait_ge(scale_step, 2)
            dve.reciprocal(scales[:, 3:4], scales[:, 2:3]).then_inc(scale_step, 1)
            dve.wait_ge(scale_step, 3)
            dve.tensor_scalar(scales[:, 3:4], scales[:, 3:4], 1.5, None, ALU.mult).then_inc(scale_step, 1)
            dve.wait_ge(scale_step, 4)
            dve.tensor_single_scalar(scales[:, 3:4].bitcast(I32), scales[:, 3:4].bitcast(I32), 0x7F800000,
                                     ALU.bitwise_and).then_inc(scale_step, 1)
            dve.wait_ge(scale_step, 5)
            dve.tensor_scalar(scales[:, 4:5], scales[:, 3:4], 2.0 ** 14, None, ALU.mult).then_inc(scale_step, 1)
            dve.tensor_scalar(scales[:, 5:6], scales[:, 3:4], 2.0 ** 14 * H_SCALE, None, ALU.mult)\
                .then_inc(scale_step, 1)
            dve.tensor_scalar(scales[:, 6:7], scales[:, 2:3], 2.0 ** -14 / H_SCALE, None, ALU.mult)\
                .then_inc(scale_step, 1)
            dve.wait_ge(vec_ready, 1)
            dve.wait_ge(scale_step, 8)
            dve.tensor_scalar(bias1_scaled[:, :, :], bias1T, scales[:, 5:6], None, ALU.mult).then_inc(scales_ready, 1)

            per_tile, per_unit = 3, 4
            per_row = NK * (NTC * per_tile + per_unit)

            with dve.Fori(0, BATCH) as b:
                for m in range(NK):
                    first = m * (NTC * per_tile + per_unit)
                    for q in range(NTC):
                        n = m * NTC + q
                        base = first + q * per_tile
                        dve.wait_ge(l0_gates, b * (NK * NTC) + (n + 1))
                        dve.scalar_tensor_tensor(gate_sum, forget[:, n % 2, :], EPS, inp[:, n % 2, :],
                                                 ALU.add, ALU.add).then_inc(l0_step, 1)
                        dve.wait_ge(l0_step, b * per_row + (base + 1))
                        dve.wait_ge(l0_forget, b * (NK * NTC) + n + 1)
                        dve.reciprocal(recip, gate_sum).then_inc(l0_recip, 1)
                        dve.wait_ge(l0_recip, b * (NK * NTC) + (n + 1))
                        dve.tensor_tensor(input_norm, inp[:, n % 2, :], recip, ALU.mult).then_inc(l0_step, 1)
                        dve.wait_ge(l0_step, b * per_row + (base + 2))
                        dve.scalar_tensor_tensor(new_info[:, q * TC:(q + 1) * TC], ps[:, n % 2, 2, :],
                                                 biasT[:, 2, m:m + 1], input_norm, ALU.add, ALU.mult)\
                            .then_inc(l0_info, 1)
                        dve.engine_nop().then_inc(l0_step, 1)
                    base = first + NTC * per_tile
                    dve.wait_ge(l0_ret, b * (NK * NTC) + (m + 1) * NTC + 1)
                    dve.tensor_tensor_scan(scaling[:, ::-1], ret[:, ::-1], ret[:, ::-1], 1.0,
                                           ALU.mult, ALU.bypass).then_inc(l0_step, 1)
                    dve.tensor_tensor_scan(prefix, ret, ret, h0T[:, bass.ds(b, 1), m],
                                           ALU.mult, ALU.bypass).then_inc(l0_step, 1)
                    dve.wait_ge(l0_step, b * per_row + (base + 1))
                    dve.wait_ge(l0_info, b * (NK * NTC) + (m + 1) * NTC + 1)
                    dve.tensor_tensor(scaling, scaling, new_info, ALU.mult).then_inc(l0_step, 1)
                    dve.wait_ge(l0_step, b * per_row + (base + 3))
                    dve.tensor_tensor_scan(hidden[:, m, :], scaling, scaling, 0.0, ALU.add, ALU.bypass)\
                        .then_inc(l0_step, 1)
                    dve.wait_ge(l0_step, b * per_row + (base + 4))
                    dve.tensor_tensor(hidden[:, m, :], hidden[:, m, :], prefix, ALU.add).then_inc(l0_x1, 1)
                dve.wait_ge(l0_products, b * (NK * NTC) + NK * NTC)
                dve.wait_ge(l0_x1, b * NK + NK + 1)
                for m in range(NK):
                    dve.tensor_tensor(xT[:, m, bass.ds(b, 1), :].rearrange("p b t -> p (b t)"),
                                      xT[:, m, bass.ds(b, 1), :].rearrange("p b t -> p (b t)"),
                                      hidden[:, m, :], ALU.add).then_inc(xw_step, 1)

            for k in range(NK):
                dve.wait_ge(wh_high, k + 1)
                dve.scalar_tensor_tensor(whp[:, k, :, 1, :],
                                         wh_f32[:, k, :].rearrange("p (n j) -> p n j", n=NMG),
                                         scales[:, 4:5],
                                         whp[:, k, :, 0, :],
                                         ALU.mult, ALU.subtract).then_inc(wh_low, 1)
            dve.memset(h_parts[:, :, :, :], 0.0).then_inc(state_zero, 1)
            dve.memset(gc[:, :, :], 0.0).then_inc(state_zero, 1)
            dve.memset(xw[:, :, :, XW_PART:XW_PART + XW_PAD], 0.0).then_inc(scale_step, 1)
            dve.memset(scrap[:, 0:1], 0.0).then_inc(pe_gates[1], HALF * NK)
            dve.memset(scrap[:, 1:2], 0.0).then_inc(act_done[1], HALF * n_act)
            dve.memset(scrap[:, 2:3], 0.0).then_inc(xs_added[1], 1)
            dve.memset(scrap[:, 3:4], 0.0).then_inc(pool_done[1], 2)
            dve.memset(scrap[:, 4:5], 0.0).then_inc(dve_done[1], HALF * n_dve)
            dve.wait_ge(h0_ready, 1)

            with dve.Fori(0, NCHUNK) as c:
                for n in range(NMG):
                    m, g = divmod(n, GATES)
                    full = pair_a[:, n % 2, :]
                    rest = pair_b[:, n % 2, :]
                    steps = BATCH * NK + c * (NMG * 4) + n * 4

                    def part(i):
                        return xw[:, m, i, 0:XW_PART].rearrange("p (t g b) -> p g b t", g=GATES, b=BATCH)[:, g]

                    def bt(ap):
                        return ap.rearrange("p (b t) -> p b t", b=BATCH)

                    dve.wait_ge(xw_full, c * NMG + (n + 1))
                    dve.tensor_tensor(bt(full)[:, :, 0], bt(full)[:, :, 0], h0_gates[:, n, :], ALU.add)\
                        .then_inc(xw_step, 1)
                    dve.wait_ge(xw_step, steps + 1)
                    dve.tensor_copy(part(0), bt(full)).then_inc(xw_step, 1)
                    dve.wait_ge(xw_step, steps + 2)
                    dve.tensor_tensor(bt(rest), bt(full), part(0), ALU.subtract).then_inc(xw_step, 1)
                    dve.wait_ge(xw_step, steps + 3)
                    dve.tensor_copy(part(1), bt(rest)).then_inc(xw_step, 1)
                    dve.wait_ge(xw_step, steps + 4)
                    dve.tensor_tensor(part(2), bt(rest), part(1), ALU.subtract).then_inc(xw_ready, 1)
                dve.memset(h0_gates[:, :, :], 0.0).then_inc(scale_step, 1)

                with dve.Fori(0, NBLOCK) as blk:
                    for t in range(BLOCK):
                        s, i = place(t)
                        now = (t + 1) % 2
                        for what, m in DVE_ORDER:
                            if what == "sum":
                                wait_gates(dve, m, t)
                                ins = dve.tensor_reduce(
                                    pre[:, m, :].rearrange("p (g b) -> p g b", b=BATCH),
                                    ps[:, s, m, i * S_COLS:(i + 1) * S_COLS]
                                    .rearrange("p (g q b) -> p g b q", q=2, b=BATCH), axis=AX.X, op=ALU.add)
                            elif what == "mul":
                                wait_act(dve, "sig", m, t)
                                ins = dve.tensor_tensor(uv[:, m, :], gc[:, m, 0:4], gc[:, m, 6:10], ALU.mult)
                            elif what == "cell":
                                wait_dve(dve, "mul", m, t)
                                ins = dve.tensor_tensor(gc[:, m, 8:10], uv[:, m, 0:2], uv[:, m, 2:4], ALU.add)
                            elif what == "high":
                                wait_act(dve, "tanh", m, t)
                                ins = dve.scalar_tensor_tensor(h_parts[:, now, m, 0:2], gc[:, m, 4:6], H_SCALE,
                                                               tanh_c[:, m, :], ALU.mult, ALU.mult)
                            elif what == "h":
                                wait_act(dve, "tanh", m, t)
                                ins = dve.tensor_tensor(h_half[:, s, m, :, i], gc[:, m, 4:6], tanh_c[:, m, :],
                                                        ALU.mult)
                            else:
                                wait_dve(dve, "high", m, t)
                                wait_dve(dve, "h", m, t)
                                ins = dve.scalar_tensor_tensor(h_parts[:, now, m, 2:4], h_half[:, s, m, :, i], H_SCALE,
                                                               h_parts[:, now, m, 0:2], ALU.mult, ALU.subtract)
                            ins.then_inc(dve_done[s], 1)
                        if i == 1:
                            wait_act(dve, "sig", 0, t)
                            dve.wait_ge(pool_done[s], 1)
                            o = 1 - s
                            dve.memset(scrap[:, 8:9], 0.0).then_inc(pe_gates[o], -HALF * NK)
                            dve.memset(scrap[:, 9:10], 0.0).then_inc(act_done[o], -HALF * n_act)
                            dve.memset(scrap[:, 10:11], 0.0).then_inc(xs_added[o], -1)
                            dve.memset(scrap[:, 11:12], 0.0).then_inc(pool_done[o], -2)
                            dve.memset(scrap[:, 12:13], 0.0).then_inc(dve_done[o], -HALF * n_dve)
                dve.wait_ge(pool_done[1], 2)
                for k in range(NK):
                    ins = dve.tensor_tensor(hist[:, k], hist[:, k], xT[:, k, :, bass.ds(c * CHUNK, CHUNK)], ALU.add)
                ins.then_inc(y_ready, 1)

        @block.tensor
        def _(pe):
            pe.wait_ge(consts, 4)
            w_stage = wh_parts[:, :].bitcast(F32)[:, 0:NW * NK * D].rearrange("p (w c d) -> p w c d", w=NW, c=NK)
            for n in range(NW * NK + BATCH * TILES):
                if n < NW * NK:
                    w, h = divmod(n, NK)
                    if h == 0:
                        pe.wait_ge(w_in[w], 16)
                    src = w_stage[:, w, h, :]
                else:
                    j, q = divmod(n - NW * NK, 4)
                    if q == 0:
                        pe.wait_ge(x_in[j], 16)
                    src = x_slots(work, j)[:, q, :]
                if n >= 8:
                    if n % 2:
                        pe.wait_ge(stored_act, (n - 8) // 2 + 1)
                    else:
                        pe.wait_ge(stored_dve, (n - 8) // 2 + 1)
                for k in range(NK):
                    ins = pe.transpose(ps8[:, n % 8, k * P:(k + 1) * P], src[:, k * P:(k + 1) * P], identf[:, :])
                ins.then_inc(turned, 1)
            tiles = NW * NK + BATCH * TILES
            pe.wait_ge(stored_act, tiles // 2)
            pe.wait_ge(stored_dve, tiles // 2)
            pe.wait_ge(small_in, 5 * 16)
            pe.transpose(ps[:, 0, 0, 0:N_VEC], vec_rows[:, :], identf[0:N_VEC, 0:N_VEC]).then_inc(vec_turned, 1)
            pe.wait_ge(vec_ready, 1)
            with pe.Fori(0, BATCH) as b:
                for n in range(NK * NTC):
                    m, q = divmod(n, NTC)
                    if n >= 2:
                        pe.wait_ge(l0_info, b * (NK * NTC) + (n - 1) + 1)
                    else:
                        pe.wait_ge(l0_info, b * (NK * NTC) + 1)
                    for w in range(NW):
                        for k in range(NK):
                            ins = pe.matmul(ps[:, n % 2, w, :], wT[:, k, w, m * P:(m + 1) * P],
                                            xT[:, k, bass.ds(b, 1), q * TC:(q + 1) * TC].rearrange("p b t -> p (b t)"),
                                            start=(k == 0), stop=(k == NK - 1))
                    ins.then_inc(l0_products, 1)
            pe.wait_ge(l0_info, BATCH * NK * NTC + 1)
            pe.wait_ge(wh_in, 16)
            for n in range(NMG):
                m, g = divmod(n, GATES)
                for k in range(NK):
                    ins = pe.matmul(ps[:, 0, 0, n * BATCH:(n + 1) * BATCH],
                                    wh_f32[:, k, g * D + m * P:g * D + (m + 1) * P], h0T[:, :, k],
                                    start=(k == 0), stop=(k == NK - 1))
            ins.then_inc(h0_product, 1)
            pe.wait_ge(wh_low, NK)
            pe.wait_ge(xw_step, BATCH * NK)
            pe.wait_ge(h0_ready, 1)
            pe.wait_ge(state_zero, 2)

            def add_inputs(s, m):
                into = ps[:, s, m, 0:HALF * S_COLS].rearrange("p (a q b) -> p a q b", q=2, b=BATCH)[:, :, 0, :]
                for i in range(NPART):
                    ins = pe.matmul(into, identb[:, :], xs[:, m, i, :], start=(i == 0), stop=True,
                                    skip_group_check=True)
                return ins

            for k in range(NK):
                pe.wait_ge(wx_in[k], 16)
            with pe.Fori(0, NCHUNK) as c:
                wait_dve(pe, "low", 3, -1)
                for n in range(NMG):
                    m, g = divmod(n, GATES)
                    if n >= 4:
                        pe.wait_ge(xw_full, c * NMG + (n - 3))
                    for k in range(NK):
                        ins = pe.matmul(ps[:, 1, n % 4, :], wx_sb[:, k, g * D + m * P:g * D + (m + 1) * P],
                                        xT[:, k, :, bass.ds(c * CHUNK, CHUNK)],
                                        start=(k == 0), stop=(k == NK - 1))
                    ins.then_inc(xw_product, 1)
                pe.wait_ge(xw_full, c * NMG + NMG)
                pe.wait_ge(y_rows, c * 4 + 1)
                pe.wait_ge(xs_first, c + 1)
                for m in range(NK):
                    ins = add_inputs(0, m)
                ins.then_inc(first_added, 1)

                with pe.Fori(0, NBLOCK) as blk:
                    for t in range(BLOCK):
                        s, i = place(t)
                        for m in ((), (0,), (1,), (2, 3))[i]:
                            if m == 0:
                                pe.wait_ge(pool_done[s], 1)
                            ins = add_inputs(1 - s, m)
                            if m == NK - 1:
                                ins.then_inc(xs_added[s], 1)
                        seen_k, seen_m = set(), set()
                        for at, (k, m) in enumerate(PE_ORDER):
                            if k not in seen_k:
                                wait_dve(pe, "low", k, t - 1)
                                seen_k.add(k)
                            if m not in seen_m:
                                if i:
                                    wait_dve(pe, "sum", m, t - 1)
                                seen_m.add(m)
                            for g in range(GATES):
                                col = i * S_COLS + g * G_COLS
                                for part in range(2):
                                    ins = pe.matmul(ps[:, s, m, col:col + G_COLS], whp[:, k, g * NK + m, part, :],
                                                    h_parts[:, t % 2, k, :], start=False, stop=(at == LAST[m]),
                                                    skip_group_check=True)
                            if at == LAST[m]:
                                ins.then_inc(pe_gates[s], 1)
                pe.wait_ge(y_ready, c + 1)
                for q in range(4):
                    b, j = divmod(q, 2)
                    for k in range(NK):
                        ins = pe.transpose(ps[:, 0, q, k * P:(k + 1) * P], hist[:, k, b, j * P:(j + 1) * P],
                                           identf[:, :])
                    ins.then_inc(y_turned, 1)


def x_slots(work, n):
    at = NK * NW * D + (n % (XSLOTS // 4)) * 4 * D
    return work[:, at:at + 4 * D].rearrange("p (j d) -> p j d", j=4)


def turned_to(wT, xT, n):
    if n < NW * NK:
        w, h = divmod(n, NK)
        return wT[:, :, w, h * P:(h + 1) * P]
    b, j = divmod(n - NW * NK, TILES)
    return xT[:, :, b, j * P:(j + 1) * P]


_INS = ['x', 'cond_1024', 'L0_cond_W_f', 'L0_cond_b_f', 'L0_cond_W_i', 'L0_cond_b_i', 'L0_cond_W_h', 'L0_cond_b_h',
        'L1_cond_Wx', 'L1_cond_Wh', 'L1_cond_b']


def kernel(**inputs):
    import numpy as _np
    import concourse.bacc as _bacc
    from concourse import mybir as _mybir
    from concourse.bass_utils import run_bass_kernel_spmd as _run

    nc = _bacc.Bacc("TRN2", target_bir_lowering=False, num_devices=1)
    arrays, args = {}, []
    for name in _INS:
        a = _np.ascontiguousarray(inputs[name])
        arrays[f"in_{name}_dram"] = a
        args.append(nc.dram_tensor(f"in_{name}_dram", a.shape, _mybir.dt.from_np(a.dtype), kind="ExternalInput").ap())
    y = nc.dram_tensor("out_dram", (BATCH, SEQ, D), _mybir.dt.float32, kind="ExternalOutput").ap()
    build(nc, *args, y)
    r = _run(nc, [arrays], core_ids=[0])
    return r.results[0]["out_dram"]
```

```python
from contextlib import ExitStack

import concourse.bass as bass
from concourse import mybir

F32 = mybir.dt.float32
F16 = mybir.dt.float16
BF16 = mybir.dt.bfloat16
I32 = mybir.dt.int32
ALU = mybir.AluOpType
ACT = mybir.ActivationFunctionType
AX = mybir.AxisListType
RMAX = bass.bass_isa.ReduceOp.max

P = 128
BATCH, SEQ, D = 2, 2048, 512
NK = D // P
GATES = 4
NMG = NK * GATES
EPS = 1e-8

TC = 512
NTC = SEQ // TC
NW = 3
TILES = SEQ // P
XSLOTS = 8

CHUNK = 256
NCHUNK = SEQ // CHUNK
HALF = 16
BLOCK = 2 * HALF
NBLOCK = CHUNK // BLOCK
XW_STEP = GATES * BATCH
XW_PART = CHUNK * XW_STEP
XW_PAD = HALF * XW_STEP
NPART = 3
N_VEC = NW * NK + NMG + BATCH * NK
OUT_FIRST = 5 * 16
H_SCALE = 4096.0
G_COLS = 2 * BATCH

CELL, OUT = 0, 1
CLASS_GATES = ((0, 1, 3), (2,))
CLASS_COLS = (3 * G_COLS, G_COLS)

PE_ORDER = [(0, 0, CELL), (0, 1, CELL), (0, 2, CELL), (1, 1, CELL), (0, 3, CELL), (0, 1, OUT),
            (1, 1, OUT), (0, 0, OUT), (1, 0, CELL), (2, 0, CELL), (1, 0, OUT), (2, 1, OUT),
            (2, 0, OUT), (3, 0, CELL), (3, 1, CELL), (2, 1, CELL), (3, 0, OUT), (2, 2, CELL),
            (3, 1, OUT), (3, 2, CELL), (1, 2, CELL), (1, 3, CELL), (2, 3, CELL), (3, 3, CELL),
            (1, 2, OUT), (3, 3, OUT), (2, 2, OUT), (2, 3, OUT), (3, 2, OUT), (1, 3, OUT), (0, 2, OUT),
            (0, 3, OUT)]
DVE_ORDER = [("sum", 0), ("sum", 1), ("mul", 0), ("sum_o", 0), ("cell", 0), ("sum_o", 1), ("mul", 1),
             ("sum", 2), ("cell", 1), ("h", 0), ("high", 0), ("low", 0), ("sum", 3), ("mul", 2),
             ("h", 1), ("high", 1), ("cell", 2), ("sum_o", 2), ("low", 1), ("mul", 3), ("sum_o", 3),
             ("cell", 3), ("h", 2), ("high", 2), ("low", 2), ("h", 3), ("high", 3), ("low", 3)]
ACT_ORDER = [("cand", 0), ("sig", 0), ("cand", 1), ("sig", 1), ("sig_o", 0), ("tanh", 0), ("sig_o", 1),
             ("sig", 2), ("cand", 2), ("tanh", 1), ("cand", 3), ("sig", 3), ("tanh", 2), ("sig_o", 2),
             ("sig_o", 3), ("tanh", 3)]
CLASSES = [(m, c) for m in range(NK) for c in (CELL, OUT)]
LAST = {mc: max(i for i, (_, *to) in enumerate(PE_ORDER) if tuple(to) == mc) for mc in CLASSES}
PE_DONE = sorted(CLASSES, key=LAST.get)
SUM_OF = {CELL: "sum", OUT: "sum_o"}


def build(nc, x, cond, w_f, b_f, w_i, b_i, w_h, b_h, wx, wh, b1, out):
    ctx = ExitStack()
    with ctx:
        def sb(name, shape, dt):
            return ctx.enter_context(nc.sbuf_tensor(name, shape, dt))

        def sem(name):
            return ctx.enter_context(nc.semaphore(name))

        xT = sb("xT", [P, NK, BATCH, SEQ], F32)
        wx_sb = sb("wx_sb", [P, NK, GATES * D], F32)
        wh_parts = sb("wh_parts", [P, NK * NMG * 2 * P], F16)
        work = sb("work", [P, NK * NPART * (XW_PART + XW_PAD) // 2], F32)
        small8 = sb("small8", [P, 2048], F32)
        pair_a = sb("pair_a", [P, 2, TC], F32)
        pair_b = sb("pair_b", [P, 2, TC], F32)
        rows8 = sb("rows8", [P, NK, D], F32)
        identf = sb("identf", [P, P], F32)
        identb = sb("identb", [P, P], BF16)
        vecT = sb("vecT", [P, N_VEC], F32)
        bias1_scaled = sb("bias1_scaled", [P, GATES, NK], F32)
        scales = sb("scales", [P, 8], F32)
        wh_tops = sb("wh_tops", [P, BATCH * NTC], F32)
        h0_gates = sb("h0_gates", [P, GATES, NK, BATCH], F32)
        h0_parts = sb("h0_parts", [P, NK, NPART, BATCH], BF16)
        h0_rest = sb("h0_rest", [P, BATCH, NK], F32)

        biasT = vecT[:, 0:NW * NK].rearrange("p (w k) -> p w k", w=NW)
        bias1T = vecT[:, NW * NK:NW * NK + NMG].rearrange("p (g m) -> p g m", g=GATES)
        h0T = vecT[:, NW * NK + NMG:N_VEC].rearrange("p (b k) -> p b k", b=BATCH)

        wT = work[:, 0:NK * NW * D].rearrange("p (k w h) -> p k w h", k=NK, w=NW)
        ret = work[:, 6144:8192]
        new_info = work[:, 8192:10240]
        scaling = work[:, 10240:12288]
        vec_rows = pair_a[0:N_VEC, 0, 0:P]
        hidden = wh_parts[:, :].bitcast(F32).rearrange("p (k t) -> p k t", k=NK)
        forget = small8[:, 0:2 * TC].rearrange("p (n t) -> p n t", n=2)
        inp = small8[:, 2 * TC:4 * TC].rearrange("p (n t) -> p n t", n=2)
        gate_sum, recip = pair_a[:, 0, :], pair_a[:, 1, :]
        forget_norm, input_norm = pair_b[:, 0, :], pair_b[:, 1, :]
        summed = rows8[:, :, :].rearrange("p a b -> p (a b)")
        wh_f32 = wx_sb

        whp = wh_parts[:, :].rearrange("p (k n s j) -> p k n s j", k=NK, n=NMG, s=2)
        xw = work[:, :].bitcast(BF16)[:, 0:NK * NPART * (XW_PART + XW_PAD)]\
            .rearrange("p (m s c) -> p m s c", m=NK, s=NPART)
        h_half = pair_b[:, :, :].rearrange("p n t -> p (n t)")[:, 0:2 * NK * BATCH * HALF]\
            .rearrange("p (s k b t) -> p s k b t", s=2, k=NK, b=BATCH)
        hist = small8[:, :].rearrange("p (k b t) -> p k b t", k=NK, b=BATCH)
        h_parts = sb("h_parts", [P, 2, NK, G_COLS], F16)
        xs = sb("xs", [P, NK, NPART, XW_PAD], BF16)
        pre = sb("pre", [P, NK, XW_STEP], F32)
        gc = sb("gc", [P, NK, (GATES + 1) * BATCH], F32)
        uv = sb("uv", [P, NK, 2 * BATCH], F32)
        tanh_c = sb("tanh_c", [P, NK, BATCH], F32)
        scrap = sb("scrap", [P, 16], F32)

        ps = ctx.enter_context(nc.psum_tensor("ps", [P, 2, NK, 512], F32))
        ps8 = ps[:, :, :, :].rearrange("p s m c -> p (s m) c")

        consts = sem("consts")
        small_in = sem("small_in")
        w_in = [sem(f"w_in{w}") for w in range(NW)]
        x_in = [sem(f"x_in{s}") for s in range(BATCH * TILES // 4)]
        wh_in = sem("wh_in")
        wx_in = [sem(f"wx_in{k}") for k in range(NK)]
        vec_turned = sem("vec_turned")
        vec_ready = sem("vec_ready")
        turned = sem("turned")
        stored_act = sem("stored_act")
        stored_dve = sem("stored_dve")
        l0_products = sem("l0_products")
        l0_gates = sem("l0_gates")
        l0_recip = sem("l0_recip")
        l0_forget = sem("l0_forget")
        l0_ret = sem("l0_ret")
        l0_info = sem("l0_info")
        l0_step = sem("l0_step")
        l0_scaling = sem("l0_scaling")
        l0_summed = sem("l0_summed")
        l0_hidden = sem("l0_hidden")
        x1_pool = sem("x1_pool")
        x1_last = sem("x1_last")
        wh_max = sem("wh_max")
        wh_max_run = sem("wh_max_run")
        h0_step = sem("h0_step")
        wh_max_all = sem("wh_max_all")
        scale_step = sem("scale_step")
        scales_ready = sem("scales_ready")
        wh_high = sem("wh_high")
        wh_low = sem("wh_low")
        h0_product = sem("h0_product")
        h0_ready = sem("h0_ready")
        state_zero = sem("state_zero")
        xw_product = sem("xw_product")
        xw_full = sem("xw_full")
        xw_step = sem("xw_step")
        xw_ready = sem("xw_ready")
        xs_first = sem("xs_first")
        pool_passed = sem("pool_passed")
        pe_passed = sem("pe_passed")
        y_ready = sem("y_ready")
        y_turned = sem("y_turned")
        y_rows = sem("y_rows")
        out_done = sem("out_done")
        pe_gates = [sem(f"pe_gates{s}") for s in range(2)]
        act_done = [sem(f"act_done{s}") for s in range(2)]
        dve_done = [sem(f"dve_done{s}") for s in range(2)]
        xs_added = [sem(f"xs_added{s}") for s in range(2)]
        pool_done = [sem(f"pool_done{s}") for s in range(2)]

        n_dve, n_act = len(DVE_ORDER), len(ACT_ORDER)

        def place(t):
            return (t % BLOCK) // HALF, t % HALF

        def wait_gates(eng, t, m, c):
            s, i = place(t)
            eng.wait_ge(pe_gates[s], i * len(CLASSES) + PE_DONE.index((m, c)) + 1)

        def wait_act(eng, t, *instructions):
            s, i = place(t)
            eng.wait_ge(act_done[s], i * n_act + max(ACT_ORDER.index(x) for x in instructions) + 1)

        def wait_dve(eng, t, *instructions):
            s, i = place(t)
            eng.wait_ge(dve_done[s], i * n_dve + max(DVE_ORDER.index(x) for x in instructions) + 1)

        block = ctx.enter_context(nc.Block())

        @block.sync
        def _(sp):
            w_stage = wh_parts[:, :].bitcast(F32)[:, 0:NW * NK * D].rearrange("p (w c d) -> p w c d", w=NW, c=NK)
            for w, src in enumerate((w_f, w_i, w_h)):
                sp.dma_start(w_stage[:, w], src.rearrange("(c p) d -> p c d", p=P)).then_inc(w_in[w], 16)
            for n in range(BATCH * TILES // 4):
                b, q = divmod(n, TILES // 4)
                if n >= XSLOTS // 4:
                    sp.wait_ge(turned, NW * NK + 4 * (n - XSLOTS // 4 + 1))
                sp.dma_start(x_slots(work, n), x[b, q * 4 * P:(q + 1) * 4 * P, :]
                             .rearrange("(j p) d -> p j d", p=P)).then_inc(x_in[n], 16)
            sp.dma_start(wh_f32[:, :, :], wh.rearrange("(k p) n -> p k n", p=P)).then_inc(wh_in, 16)
            for k in range(NK):
                sp.wait_ge(wh_low, k + 1)
                sp.dma_start(wx_sb[:, k, :], wx[k * P:(k + 1) * P, :]).then_inc(wx_in[k], 16)
            with sp.Fori(1, NCHUNK + 1) as c:
                for q in range(4):
                    b, j = divmod(q, 2)
                    sp.wait_ge(y_rows, c * 4 + (q + 1))
                    sp.dma_start(out[b, bass.ds((c - 1) * CHUNK + j * P, P), :], rows8[:, q, :]).then_inc(out_done, 16)
            sp.wait_ge(out_done, OUT_FIRST + NCHUNK * 4 * 16)

        @block.gpsimd
        def _(pool):
            for counted in (l0_ret, l0_info, l0_scaling):
                pool.sem_inc(counted, 1)
            pool.sem_inc(x1_pool, NK - 1)
            pool.sem_inc(out_done, OUT_FIRST)
            pool.memset(identf[:, :], 0.0).then_inc(consts, 1)
            pool.memset(identb[:, :], 0.0).then_inc(consts, 1)
            pool.wait_ge(consts, 2)
            for ident in (identf, identb):
                pool.affine_select(out=ident[:, :], in_=ident[:, :], compare_op=ALU.not_equal, fill=1.0,
                                   base=0, pattern=[[-1, P]], channel_multiplier=1).then_inc(consts, 1)
            with pool.Fori(0, BATCH) as b:
                pool.wait_ge(wh_max, b + 1)
                pool.sem_inc(pool_passed, 1)
                pool.partition_all_reduce(scales[:, 2:3], scales[:, 7:8], P, RMAX).then_inc(wh_max_all, 1)
                for m in range(NK - 1):
                    pool.wait_ge(l0_summed, b * NK + (m + 1))
                    pool.tensor_tensor(hidden[:, m, :], hidden[:, m, :], summed, ALU.add).then_inc(l0_hidden, 1)
                pool.wait_ge(l0_products, b * (NK * NTC) + NK * NTC)
                for m in range(NK - 1):
                    pool.wait_ge(l0_hidden, b * (NK - 1) + (m + 1))
                    x_row = xT[:, m, bass.ds(b, 1), :].rearrange("p b t -> p (b t)")
                    pool.tensor_tensor(x_row, x_row, hidden[:, m, :], ALU.add).then_inc(x1_pool, 1)
            with pool.Fori(0, NCHUNK) as c:
                pool.wait_ge(y_turned, c * 4 + 4)
                pool.sem_inc(pool_passed, 1)
                with pool.Fori(0, NBLOCK) as blk:
                    for s in range(2):
                        pool.wait_ge(xs_added[s], 1)
                        pool.tensor_copy(xs[:, :, :, :], xw[:, :, :, bass.ds(blk * (2 * XW_PAD) + (1 + s) * XW_PAD, XW_PAD)])\
                            .then_inc(pool_done[s], 1)
                        wait_dve(pool, s * HALF + HALF - 1, *(("h", m) for m in range(NK)))
                        pool.tensor_copy(hist[:, :, :, bass.ds(blk * BLOCK + s * HALF, HALF)],
                                         h_half[:, s]).then_inc(pool_done[s], 1)

        @block.scalar
        def _(act):
            for at, src in ((0, b_f), (NK, b_i), (2 * NK, b_h), (NW * NK, b1)):
                rows = src.shape[0] // P
                act.dma_start(vec_rows[at:at + rows, :], src.rearrange("(k p) -> k p", p=P)).then_inc(small_in, 16)
            act.dma_start(vec_rows[NW * NK + NMG:N_VEC, :], cond.rearrange("b (k p) -> (b k) p", p=P))\
               .then_inc(small_in, 16)
            for n in range(1, NW * NK + BATCH * TILES, 2):
                act.wait_ge(turned, n + 1)
                act.activation(turned_to(wT, xT, n), ps8[:, n % 8, :].rearrange("p (k t) -> p k t", k=NK),
                               ACT.Copy).then_inc(stored_act, 1)
            act.wait_ge(vec_turned, 1)
            act.activation(vecT[:, :], ps[:, 0, 0, 0:N_VEC], ACT.Copy).then_inc(vec_ready, 1)
            act.wait_ge(vec_ready, 1)
            with act.Fori(0, BATCH) as b:
                for n in range(NK * NTC):
                    m, q = divmod(n, NTC)
                    act.wait_ge(l0_products, b * (NK * NTC) + (n + 1))
                    if n >= 2:
                        act.wait_ge(l0_info, b * (NK * NTC) + (n - 1) + 1)
                    else:
                        act.wait_ge(l0_info, b * (NK * NTC) + 1)
                    act.activation(forget[:, n % 2, :], ps[:, n % 2, 0, :], ACT.Sigmoid, bias=biasT[:, 0, m:m + 1])
                    act.activation(inp[:, n % 2, :], ps[:, n % 2, 1, :], ACT.Sigmoid, bias=biasT[:, 1, m:m + 1])\
                        .then_inc(l0_gates, 1)
                    act.wait_ge(l0_forget, b * (NK * NTC) + (n + 1))
                    if q == 0:
                        act.wait_ge(l0_scaling, b * NK + m + 1)
                    act.activation(ret[:, q * TC:(q + 1) * TC], forget_norm, ACT.Copy, bias=EPS).then_inc(l0_ret, 1)
            act.wait_ge(scales_ready, BATCH)
            for k in range(NK):
                if k < NK - 1:
                    act.wait_ge(x1_pool, BATCH * (NK - 1) + k + 1)
                else:
                    act.wait_ge(x1_last, BATCH)
                act.activation(whp[:, k, :, 0, :],
                               wh_f32[:, k, :].rearrange("p (n j) -> p n j", n=NMG),
                               ACT.Copy, scale=scales[:, 4:5]).then_inc(wh_high, 1)
            unscale = act.alloc_register("unscale")
            act.reg_load(unscale, scales[0:1, 6:7].bitcast(I32))
            act.wait_ge(state_zero, 2)

            def copy_rows(counted, last_stored):
                act.wait_ge(out_done, last_stored)
                for q in range(4):
                    act.wait_ge(y_turned, counted + (q + 1))
                    act.activation(rows8[:, q, :], ps[:, 0, q, :], ACT.Copy).then_inc(y_rows, 1)

            with act.Fori(0, NCHUNK) as c:
                for n in range(NMG):
                    act.wait_ge(xw_product, c * NMG + (n + 1))
                    if n >= 2:
                        act.wait_ge(xw_ready, c * NMG + (n - 1))
                    act.activation(pair_a[:, n % 2, :], ps[:, 1, n % 4, :], ACT.Identity,
                                   bias=bias1_scaled[:, n % GATES, n // GATES:n // GATES + 1],
                                   scale=scales[:, 5:6]).then_inc(xw_full, 1)
                copy_rows(c * 4, c * (4 * 16) + 16)
                with act.Fori(0, NBLOCK) as blk:
                    for t in range(BLOCK):
                        done = act_done[place(t)[0]]
                        for what, m in ACT_ORDER:
                            if what == "cand":
                                wait_dve(act, t, ("sum", m))
                                act.activation(gc[:, m, 6:8], pre[:, m, 4:6], ACT.Tanh, scale=unscale)\
                                    .then_inc(done, 1)
                            elif what == "sig":
                                wait_dve(act, t, ("sum", m))
                                act.activation(gc[:, m, 0:4], pre[:, m, 0:4], ACT.Sigmoid, scale=unscale)\
                                    .then_inc(done, 1)
                            elif what == "sig_o":
                                wait_dve(act, t, ("sum_o", m))
                                act.activation(gc[:, m, 4:6], pre[:, m, 6:8], ACT.Sigmoid, scale=unscale)\
                                    .then_inc(done, 1)
                            else:
                                wait_dve(act, t, ("cell", m))
                                act.activation(tanh_c[:, m, :], gc[:, m, 8:10], ACT.Tanh).then_inc(done, 1)
            copy_rows(NCHUNK * 4, NCHUNK * 4 * 16 + 16)

        @block.vector
        def _(dve):
            for n in range(0, NW * NK + BATCH * TILES, 2):
                dve.wait_ge(turned, n + 1)
                dve.tensor_copy(turned_to(wT, xT, n), ps8[:, n % 8, :].rearrange("p (k t) -> p k t", k=NK))\
                    .then_inc(stored_dve, 1)
            dve.wait_ge(vec_ready, 1)
            h0_part = [h0_parts[:, :, i, :].rearrange("p k b -> p b k") for i in range(NPART)]
            dve.tensor_copy(h0_part[0], h0T).then_inc(h0_step, 1)
            dve.wait_ge(h0_step, 1)
            dve.tensor_tensor(h0_rest[:, :, :], h0T, h0_part[0], ALU.subtract).then_inc(h0_step, 1)
            dve.wait_ge(h0_step, 2)
            dve.tensor_copy(h0_part[1], h0_rest[:, :, :]).then_inc(h0_step, 1)
            dve.wait_ge(h0_step, 3)
            dve.tensor_tensor(h0_part[2], h0_rest[:, :, :], h0_part[1], ALU.subtract).then_inc(h0_step, 1)
            def wh_top(b, q):
                cols = GATES * D * (NK // BATCH) // NTC
                k, part = divmod(q * cols, GATES * D)
                dve.wait_ge(wh_in, 16)
                dve.wait_ge(wh_max_run, b * NTC + (q + 1))
                dve.tensor_reduce(wh_tops[:, bass.ds(b * NTC + q, 1)],
                                  wh_f32[:, bass.ds(b * (NK // BATCH) + k, 1), part:part + cols],
                                  axis=AX.XY, op=ALU.max, apply_absolute_value=True).then_inc(wh_max_run, 1)
                if q == NTC - 1:
                    dve.wait_ge(wh_max_run, b * NTC + NTC + 1)
                    dve.tensor_reduce(scales[:, 7:8], wh_tops[:, :], axis=AX.X, op=ALU.max).then_inc(wh_max, 1)

            def run_sum(b, m):
                dve.wait_ge(l0_step, b * per_row + ((m + 1) * (NTC * per_tile + per_unit)))
                if m:
                    dve.wait_ge(l0_hidden, b * (NK - 1) + m)
                dve.tensor_tensor_scan(summed, scaling, scaling, 0.0, ALU.add, ALU.bypass).then_inc(l0_summed, 1)

            def find_scales(b):
                dve.wait_ge(wh_max_all, b + 1)
                dve.tensor_scalar(scales[:, 2:3], scales[:, 2:3], 2.0 ** -46, 2.0 ** 100, ALU.max, ALU.min)\
                    .then_inc(scale_step, 1)
                dve.wait_ge(scale_step, b * 8 + 1)
                dve.tensor_single_scalar(scales[:, 2:3].bitcast(I32), scales[:, 2:3].bitcast(I32), 0x7F800000,
                                         ALU.bitwise_and).then_inc(scale_step, 1)
                dve.wait_ge(scale_step, b * 8 + 2)
                dve.reciprocal(scales[:, 3:4], scales[:, 2:3]).then_inc(scale_step, 1)
                dve.wait_ge(scale_step, b * 8 + 3)
                dve.tensor_scalar(scales[:, 3:4], scales[:, 3:4], 1.5, None, ALU.mult).then_inc(scale_step, 1)
                dve.wait_ge(scale_step, b * 8 + 4)
                dve.tensor_single_scalar(scales[:, 3:4].bitcast(I32), scales[:, 3:4].bitcast(I32), 0x7F800000,
                                         ALU.bitwise_and).then_inc(scale_step, 1)
                dve.wait_ge(scale_step, b * 8 + 5)
                dve.tensor_scalar(scales[:, 4:5], scales[:, 3:4], 2.0 ** 14, None, ALU.mult).then_inc(scale_step, 1)
                dve.tensor_scalar(scales[:, 5:6], scales[:, 3:4], 2.0 ** 14 * H_SCALE, None, ALU.mult)\
                    .then_inc(scale_step, 1)
                dve.tensor_scalar(scales[:, 6:7], scales[:, 2:3], 2.0 ** -14 / H_SCALE, None, ALU.mult)\
                    .then_inc(scale_step, 1)
                dve.wait_ge(scale_step, b * 8 + 8)
                dve.tensor_scalar(bias1_scaled[:, :, :], bias1T, scales[:, 5:6], None, ALU.mult).then_inc(scales_ready, 1)

            per_tile, per_unit = 3, 1
            per_row = NK * (NTC * per_tile + per_unit) + 1
            dve.memset(wh_tops[:, :], 0.0).then_inc(wh_max_run, 1)
            with dve.Fori(0, BATCH) as b:
                for m in range(NK):
                    first = m * (NTC * per_tile + per_unit)
                    for q in range(NTC):
                        n = m * NTC + q
                        at = slice(q * TC, (q + 1) * TC)
                        base = first + q * per_tile
                        dve.wait_ge(l0_gates, b * (NK * NTC) + (n + 1))
                        dve.scalar_tensor_tensor(gate_sum, forget[:, n % 2, :], EPS, inp[:, n % 2, :],
                                                 ALU.add, ALU.add).then_inc(l0_step, 1)
                        dve.wait_ge(l0_step, b * per_row + (base + 1))
                        dve.reciprocal(recip, gate_sum).then_inc(l0_recip, 1)
                        dve.wait_ge(l0_recip, b * (NK * NTC) + (n + 1))
                        dve.wait_ge(l0_ret, b * (NK * NTC) + n + 1)
                        dve.tensor_tensor(forget_norm, forget[:, n % 2, :], recip, ALU.mult).then_inc(l0_forget, 1)
                        dve.tensor_tensor(input_norm, inp[:, n % 2, :], recip, ALU.mult).then_inc(l0_step, 1)
                        dve.wait_ge(l0_step, b * per_row + (base + 2))
                        dve.scalar_tensor_tensor(new_info[:, at], ps[:, n % 2, 2, :],
                                                 biasT[:, 2, m:m + 1], input_norm, ALU.add, ALU.mult)\
                            .then_inc(l0_info, 1)
                        dve.wait_ge(l0_ret, b * (NK * NTC) + (n + 1) + 1)
                        if q:
                            dve.wait_ge(l0_step, b * per_row + base)
                        elif m < NK - 1:
                            dve.wait_ge(x1_pool, b * (NK - 1) + (m + 1))
                        before = hidden[:, m, q * TC - 1:q * TC] if q else h0T[:, bass.ds(b, 1), m]
                        dve.tensor_tensor_scan(hidden[:, m, at], ret[:, at], ret[:, at], before,
                                               ALU.mult, ALU.bypass).then_inc(l0_step, 1)
                        if m == 0:
                            wh_top(b, q)
                        elif q == 0:
                            run_sum(b, m - 1)
                    base = first + NTC * per_tile
                    dve.tensor_tensor_scan(scaling[:, ::-1], ret[:, ::-1], ret[:, ::-1], 1.0,
                                           ALU.mult, ALU.bypass).then_inc(l0_scaling, 1)
                    dve.wait_ge(l0_scaling, b * NK + (m + 1) + 1)
                    dve.wait_ge(l0_info, b * (NK * NTC) + (m + 1) * NTC + 1)
                    dve.tensor_tensor(scaling, scaling, new_info, ALU.mult).then_inc(l0_step, 1)
                    if m == NK - 2:
                        find_scales(b)
                run_sum(b, NK - 1)
                dve.wait_ge(l0_summed, b * NK + NK)
                dve.tensor_tensor(hidden[:, NK - 1, :], hidden[:, NK - 1, :], summed, ALU.add).then_inc(l0_step, 1)
                dve.wait_ge(l0_step, b * per_row + per_row)
                dve.wait_ge(l0_products, b * (NK * NTC) + NK * NTC)
                x_row = xT[:, NK - 1, bass.ds(b, 1), :].rearrange("p b t -> p (b t)")
                dve.tensor_tensor(x_row, x_row, hidden[:, NK - 1, :], ALU.add).then_inc(x1_last, 1)

            for k in range(NK):
                dve.wait_ge(wh_high, k + 1)
                dve.scalar_tensor_tensor(whp[:, k, :, 1, :],
                                         wh_f32[:, k, :].rearrange("p (n j) -> p n j", n=NMG),
                                         scales[:, 4:5],
                                         whp[:, k, :, 0, :],
                                         ALU.mult, ALU.subtract).then_inc(wh_low, 1)
            dve.memset(h_parts[:, :, :, :], 0.0).then_inc(state_zero, 1)
            dve.memset(gc[:, :, :], 0.0).then_inc(state_zero, 1)
            dve.memset(hist[:, :, :, :], 0.0).then_inc(y_ready, 1)
            dve.memset(xw[:, :, :, XW_PART:XW_PART + XW_PAD], 0.0).then_inc(scale_step, 1)
            dve.memset(scrap[:, 0:1], 0.0).then_inc(pe_gates[1], HALF * len(CLASSES))
            dve.memset(scrap[:, 1:2], 0.0).then_inc(act_done[1], HALF * n_act)
            dve.memset(scrap[:, 2:3], 0.0).then_inc(xs_added[1], 1)
            dve.memset(scrap[:, 3:4], 0.0).then_inc(pool_done[1], 2)
            dve.memset(scrap[:, 4:5], 0.0).then_inc(dve_done[1], HALF * n_dve)
            dve.wait_ge(h0_product, 1)
            dve.tensor_reduce(h0_gates[:, :, :, :], ps[:, 0, 0, 0:NMG * NPART * BATCH]
                              .rearrange("p (g m i b) -> p g m b i", g=GATES, m=NK, i=NPART),
                              axis=AX.X, op=ALU.add).then_inc(h0_step, 1)
            dve.wait_ge(h0_step, 5)
            dve.tensor_scalar(h0_gates[:, :, :, :], h0_gates[:, :, :, :], H_SCALE, None, ALU.mult)\
               .then_inc(h0_ready, 1)
            dve.wait_ge(h0_ready, 1)

            with dve.Fori(0, NCHUNK) as c:
                for n in range(NMG):
                    m, g = divmod(n, GATES)
                    full = pair_a[:, n % 2, :]
                    rest = pair_b[:, n % 2, :]
                    steps = c * (NMG * 4) + n * 4

                    def part(i):
                        at = (CLASS_GATES[CELL] + CLASS_GATES[OUT]).index(g)
                        return xw[:, m, i, 0:XW_PART].rearrange("p (t g b) -> p g b t", g=GATES, b=BATCH)[:, at]

                    def bt(ap):
                        return ap.rearrange("p (b t) -> p b t", b=BATCH)

                    dve.wait_ge(xw_full, c * NMG + (n + 1))
                    dve.tensor_tensor(bt(full)[:, :, 0], bt(full)[:, :, 0], h0_gates[:, g, m, :], ALU.add)\
                        .then_inc(xw_step, 1)
                    dve.wait_ge(xw_step, steps + 1)
                    dve.tensor_copy(part(0), bt(full)).then_inc(xw_step, 1)
                    dve.wait_ge(xw_step, steps + 2)
                    dve.tensor_tensor(bt(rest), bt(full), part(0), ALU.subtract).then_inc(xw_step, 1)
                    dve.wait_ge(xw_step, steps + 3)
                    dve.tensor_copy(part(1), bt(rest)).then_inc(xw_step, 1)
                    dve.wait_ge(xw_step, steps + 4)
                    dve.tensor_tensor(part(2), bt(rest), part(1), ALU.subtract).then_inc(xw_ready, 1)
                    if g == GATES - 1:
                        dve.wait_ge(xw_ready, c * NMG + (n + 1))
                        dve.tensor_copy(xs[:, m, :, :], xw[:, m, :, 0:XW_PAD]).then_inc(xs_first, 1)
                dve.memset(h0_gates[:, :, :, :], 0.0).then_inc(scale_step, 1)

                with dve.Fori(0, NBLOCK) as blk:
                    for t in range(BLOCK):
                        s, i = place(t)
                        now = (t + 1) % 2
                        for what, m in DVE_ORDER:
                            if what in ("sum", "sum_o"):
                                cls = CELL if what == "sum" else OUT
                                into = pre[:, m, 0:6] if what == "sum" else pre[:, m, 6:8]
                                wait_gates(dve, t, m, cls)
                                ins = dve.tensor_reduce(
                                    into.rearrange("p (g b) -> p g b", b=BATCH),
                                    ps[:, cls, m, i * CLASS_COLS[cls]:(i + 1) * CLASS_COLS[cls]]
                                    .rearrange("p (g q b) -> p g b q", q=2, b=BATCH), axis=AX.X, op=ALU.add)
                            elif what == "mul":
                                wait_act(dve, t, ("sig", m), ("cand", m))
                                ins = dve.tensor_tensor(uv[:, m, :], gc[:, m, 0:4], gc[:, m, 6:10], ALU.mult)
                            elif what == "cell":
                                wait_dve(dve, t, ("mul", m))
                                ins = dve.tensor_tensor(gc[:, m, 8:10], uv[:, m, 0:2], uv[:, m, 2:4], ALU.add)
                            elif what == "high":
                                wait_act(dve, t, ("sig_o", m), ("tanh", m))
                                ins = dve.scalar_tensor_tensor(h_parts[:, now, m, 0:2], gc[:, m, 4:6], H_SCALE,
                                                               tanh_c[:, m, :], ALU.mult, ALU.mult)
                            elif what == "h":
                                wait_act(dve, t, ("sig_o", m), ("tanh", m))
                                ins = dve.tensor_tensor(h_half[:, s, m, :, i], gc[:, m, 4:6], tanh_c[:, m, :],
                                                        ALU.mult)
                            else:
                                wait_dve(dve, t, ("high", m), ("h", m))
                                ins = dve.scalar_tensor_tensor(h_parts[:, now, m, 2:4], h_half[:, s, m, :, i], H_SCALE,
                                                               h_parts[:, now, m, 0:2], ALU.mult, ALU.subtract)
                            ins.then_inc(dve_done[s], 1)
                        if i == 1:
                            o = 1 - s
                            dve.wait_ge(pool_done[o], 2)
                            wait_act(dve, t, ("sig", 0))
                            dve.memset(scrap[:, 8:9], 0.0).then_inc(pe_gates[o], -HALF * len(CLASSES))
                            dve.memset(scrap[:, 9:10], 0.0).then_inc(act_done[o], -HALF * n_act)
                            dve.memset(scrap[:, 10:11], 0.0).then_inc(xs_added[o], -1)
                            dve.memset(scrap[:, 11:12], 0.0).then_inc(pool_done[o], -2)
                            dve.memset(scrap[:, 12:13], 0.0).then_inc(dve_done[o], -HALF * n_dve)
                dve.wait_ge(pool_done[1], 2)
                for k in range(NK):
                    ins = dve.tensor_tensor(hist[:, k], hist[:, k], xT[:, k, :, bass.ds(c * CHUNK, CHUNK)], ALU.add)
                ins.then_inc(y_ready, 1)

        @block.tensor
        def _(pe):
            pe.wait_ge(consts, 4)
            w_stage = wh_parts[:, :].bitcast(F32)[:, 0:NW * NK * D].rearrange("p (w c d) -> p w c d", w=NW, c=NK)
            for n in range(NW * NK + BATCH * TILES):
                if n < NW * NK:
                    w, h = divmod(n, NK)
                    if h == 0:
                        pe.wait_ge(w_in[w], 16)
                    src = w_stage[:, w, h, :]
                else:
                    j, q = divmod(n - NW * NK, 4)
                    if q == 0:
                        pe.wait_ge(x_in[j], 16)
                    src = x_slots(work, j)[:, q, :]
                if n >= 8:
                    if n % 2:
                        pe.wait_ge(stored_act, (n - 8) // 2 + 1)
                    else:
                        pe.wait_ge(stored_dve, (n - 8) // 2 + 1)
                for k in range(NK):
                    ins = pe.transpose(ps8[:, n % 8, k * P:(k + 1) * P], src[:, k * P:(k + 1) * P], identf[:, :])
                ins.then_inc(turned, 1)
            tiles = NW * NK + BATCH * TILES
            pe.wait_ge(stored_act, tiles // 2)
            pe.wait_ge(stored_dve, tiles // 2)
            pe.wait_ge(small_in, 5 * 16)
            pe.transpose(ps[:, 0, 0, 0:N_VEC], vec_rows, identf[0:N_VEC, 0:N_VEC]).then_inc(vec_turned, 1)
            pe.wait_ge(vec_ready, 1)
            with pe.Fori(0, BATCH) as b:
                for n in range(NK * NTC):
                    m, q = divmod(n, NTC)
                    if n >= 2:
                        pe.wait_ge(l0_info, b * (NK * NTC) + (n - 1) + 1)
                    else:
                        pe.wait_ge(l0_info, b * (NK * NTC) + 1)
                    for w in range(NW):
                        for k in range(NK):
                            ins = pe.matmul(ps[:, n % 2, w, :], wT[:, k, w, m * P:(m + 1) * P],
                                            xT[:, k, bass.ds(b, 1), q * TC:(q + 1) * TC].rearrange("p b t -> p (b t)"),
                                            start=(k == 0), stop=(k == NK - 1))
                    ins.then_inc(l0_products, 1)
            pe.wait_ge(l0_info, BATCH * NK * NTC + 1)
            pe.wait_ge(h0_step, 4)
            for n in range(NMG):
                into = ps[:, 0, 0, n * NPART * BATCH:(n + 1) * NPART * BATCH]
                for k in range(NK):
                    if n == 0:
                        pe.wait_ge(wh_low, k + 1)
                    for part in range(2):
                        ins = pe.matmul(into, whp[:, k, n, part, :], h0_parts[:, k, :, :],
                                        start=(k == 0 and part == 0), stop=(k == NK - 1 and part == 1))
            ins.then_inc(h0_product, 1)
            pe.wait_ge(x1_pool, (BATCH + 1) * (NK - 1))
            pe.wait_ge(x1_last, BATCH)
            pe.wait_ge(state_zero, 2)

            def add_inputs(m, cls):
                into = ps[:, cls, m, 0:HALF * CLASS_COLS[cls]]\
                    .rearrange("p (t g q b) -> p t g q b", t=HALF, q=2, b=BATCH)[:, :, :, 0, :]
                for i in range(NPART):
                    src = xs[:, m, i, :].rearrange("p (t g b) -> p t g b", g=GATES, b=BATCH)
                    src = src[:, :, 0:3, :] if cls == CELL else src[:, :, 3:4, :]
                    ins = pe.matmul(into, identb[:, :], src, start=(i == 0), stop=True, skip_group_check=True)
                return ins

            def turn_rows(made):
                pe.wait_ge(y_ready, made)
                for q in range(4):
                    b, j = divmod(q, 2)
                    for k in range(NK):
                        ins = pe.transpose(ps[:, 0, q, k * P:(k + 1) * P], hist[:, k, b, j * P:(j + 1) * P],
                                           identf[:, :])
                    ins.then_inc(y_turned, 1)

            for k in range(NK):
                pe.wait_ge(wx_in[k], 16)
            pe.wait_ge(h0_ready, 1)
            with pe.Fori(0, NCHUNK) as c:
                for n in range(NMG):
                    m, g = divmod(n, GATES)
                    if n >= 4:
                        pe.wait_ge(xw_full, c * NMG + (n - 3))
                    else:
                        wait_dve(pe, -1, ("sum_o", n))
                    for k in range(NK):
                        ins = pe.matmul(ps[:, 1, n % 4, :], wx_sb[:, k, g * D + m * P:g * D + (m + 1) * P],
                                        xT[:, k, :, bass.ds(c * CHUNK, CHUNK)],
                                        start=(k == 0), stop=(k == NK - 1))
                    ins.then_inc(xw_product, 1)
                turn_rows(c + 1)
                pe.wait_ge(xw_full, c * NMG + NMG)
                pe.wait_ge(y_rows, c * 4 + 4)
                pe.wait_ge(xs_first, c * NK + NK)
                pe.sem_inc(pe_passed, 1)

                with pe.Fori(0, NBLOCK) as blk:
                    for t in range(BLOCK):
                        s, i = place(t)
                        seen_k, seen_mc, waited = set(), set(), -1
                        for at, (k, m, cls) in enumerate(PE_ORDER):
                            waits = [("low", k)] if k not in seen_k else []
                            if (m, cls) not in seen_mc:
                                waits.append((SUM_OF[cls], m))
                            newest = max([DVE_ORDER.index(w) for w in waits], default=-1)
                            if newest > waited:
                                wait_dve(pe, t - 1, *waits)
                                waited = newest
                            if i == 0 and (m, cls) not in seen_mc:
                                if not seen_mc:
                                    pe.wait_ge(pool_done[1 - s], 1)
                                ins = add_inputs(m, cls)
                                if len(seen_mc) == len(CLASSES) - 1:
                                    ins.then_inc(xs_added[s], 1)
                            seen_k.add(k)
                            seen_mc.add((m, cls))
                            for j, g in enumerate(CLASS_GATES[cls]):
                                col = i * CLASS_COLS[cls] + j * G_COLS
                                for part in range(2):
                                    ins = pe.matmul(ps[:, cls, m, col:col + G_COLS], whp[:, k, g * NK + m, part, :],
                                                    h_parts[:, t % 2, k, :], start=False, stop=(at == LAST[m, cls]),
                                                    skip_group_check=True)
                            if at == LAST[m, cls]:
                                ins.then_inc(pe_gates[s], 1)
            turn_rows(NCHUNK + 1)


def x_slots(work, n):
    at = NK * NW * D + (n % (XSLOTS // 4)) * 4 * D
    return work[:, at:at + 4 * D].rearrange("p (j d) -> p j d", j=4)


def turned_to(wT, xT, n):
    if n < NW * NK:
        w, h = divmod(n, NK)
        return wT[:, :, w, h * P:(h + 1) * P]
    b, j = divmod(n - NW * NK, TILES)
    return xT[:, :, b, j * P:(j + 1) * P]


_INS = ['x', 'cond_1024', 'L0_cond_W_f', 'L0_cond_b_f', 'L0_cond_W_i', 'L0_cond_b_i', 'L0_cond_W_h', 'L0_cond_b_h',
        'L1_cond_Wx', 'L1_cond_Wh', 'L1_cond_b']


def kernel(**inputs):
    import numpy as _np
    import concourse.bacc as _bacc
    from concourse import mybir as _mybir
    from concourse.bass_utils import run_bass_kernel_spmd as _run

    nc = _bacc.Bacc("TRN2", target_bir_lowering=False, num_devices=1)
    arrays, args = {}, []
    for name in _INS:
        a = _np.ascontiguousarray(inputs[name])
        arrays[f"in_{name}_dram"] = a
        args.append(nc.dram_tensor(f"in_{name}_dram", a.shape, _mybir.dt.from_np(a.dtype), kind="ExternalInput").ap())
    y = nc.dram_tensor("out_dram", (BATCH, SEQ, D), _mybir.dt.float32, kind="ExternalOutput").ap()
    build(nc, *args, y)
    r = _run(nc, [arrays], core_ids=[0])
    return r.results[0]["out_dram"]
```
